# Optimizing a Trainium2 kernel written in Bass

```python
import numpy as np
import jax
import jax.numpy as jnp

def _softmax(x, axis=-1):
    return jax.nn.softmax(x, axis=axis)

def _gelu(x):
    return jax.nn.gelu(x, approximate=True)

def _silu(x):
    return jax.nn.silu(x)

def _sigmoid(x):
    return jax.nn.sigmoid(x)

def _layernorm(x, axis=-1, eps=1e-05):
    m = jnp.mean(x, axis=axis, keepdims=True)
    v = jnp.var(x, axis=axis, keepdims=True)
    return (x - m) / jnp.sqrt(v + eps)

def _scatter_add(tgt, idx, src, axis=0):
    return tgt.at[idx].add(src)

def _segment_sum(src, seg, n):
    return jax.ops.segment_sum(src, seg, n)
kernel_name = 'mk_seq_postln_d1_jaxref_r4_fb92c7'

def setup_inputs(seed: int=0):
    np.random.seed(seed)
    _w = jnp.asarray

    def _L0_attn_setup():
        import jax, jax.numpy as jnp
        import numpy as np
        FP32_EPS = 1.1920929e-07

        def rms_norm(x):
            return x * jax.lax.rsqrt(jnp.mean(x * x, axis=-1, keepdims=True) + FP32_EPS)
        key = jax.random.key(seed)
        k1, k2, k3, k4 = jax.random.split(key, 4)
        n_embd, n_qkv = (256, 256)
        B, T = (4, 2048)

        def casted_init(k, out_f, in_f):
            s = 3.0 ** 0.5 * in_f ** (-0.5)
            return jax.random.uniform(k, (out_f, in_f), jnp.float32, -s, s)
        return {'x': jax.random.normal(k1, (B, T, n_embd), jnp.float32), 'w_qkv': casted_init(k2, 3 * n_qkv, n_embd), 'w_swiglu': casted_init(k3, 2 * n_embd, n_qkv), 'w_out': casted_init(k4, n_embd, n_embd)}
    _L0_attn_in = _L0_attn_setup()

    def _L0_ffn_setup():
        import jax, jax.numpy as jnp
        import numpy as np
        DIM = 256
        HIDDEN = 768
        SCALE = 1.0 / 127.0

        def _dequant(w_int, dtype):
            return w_int.astype(dtype) * jnp.asarray(SCALE, dtype)
        key = jax.random.key(seed)
        k_x, k_g, k_u, k_d = jax.random.split(key, 4)
        x = jax.random.normal(k_x, (4, 512, DIM), dtype=jnp.float32)
        w_gate = jax.random.randint(k_g, (HIDDEN, DIM), -127, 128, dtype=jnp.int32)
        w_up = jax.random.randint(k_u, (HIDDEN, DIM), -127, 128, dtype=jnp.int32)
        w_down = jax.random.randint(k_d, (DIM, HIDDEN), -127, 128, dtype=jnp.int32)
        return {'x': x, 'w_gate': w_gate, 'w_up': w_up, 'w_down': w_down}
    _L0_ffn_in = _L0_ffn_setup()
    _d = {'L0_attn_x': _L0_attn_in['x'], 'L0_attn_w_qkv': _L0_attn_in['w_qkv'], 'L0_attn_w_swiglu': _L0_attn_in['w_swiglu'], 'L0_attn_w_out': _L0_attn_in['w_out'], 'L0_ffn_w_gate': _L0_ffn_in['w_gate'], 'L0_ffn_w_up': _L0_ffn_in['w_up'], 'L0_ffn_w_down': _L0_ffn_in['w_down']}
    _x0 = _d['L0_attn_x']
    _d['L0_attn_x'] = jax.random.normal(jax.random.fold_in(jax.random.key(seed), 1), (8, 1024, 256), dtype=_x0.dtype)
    del _x0
    return _d

def reference(L0_attn_x, L0_attn_w_qkv, L0_attn_w_swiglu, L0_attn_w_out, L0_ffn_w_gate, L0_ffn_w_up, L0_ffn_w_down):

    def _L0_attn_ref(x, w_qkv, w_swiglu, w_out):
        import jax, jax.numpy as jnp
        import numpy as np
        FP32_EPS = 1.1920929e-07

        def rms_norm(x):
            return x * jax.lax.rsqrt(jnp.mean(x * x, axis=-1, keepdims=True) + FP32_EPS)
        qkv = jnp.einsum('btd,ed->bte', rms_norm(x), w_qkv)
        q, k, v = jnp.split(qkv, 3, axis=-1)
        q = rms_norm(q)
        k = rms_norm(k)
        w = jnp.exp(k)
        kv = w * v
        w = jnp.cumsum(w, axis=1)
        kv = jnp.cumsum(kv, axis=1)
        y = kv / (w + 1e-06)
        y = jax.nn.sigmoid(q) * y
        uv = jnp.einsum('bte,fe->btf', y, w_swiglu)
        u, g = jnp.split(uv, 2, axis=-1)
        return x + jnp.einsum('btd,ed->bte', u * jax.nn.silu(g), w_out)

    def _L0_ffn_ref(x, w_gate, w_up, w_down):
        import jax, jax.numpy as jnp
        import numpy as np
        DIM = 256
        HIDDEN = 768
        SCALE = 1.0 / 127.0

        def _dequant(w_int, dtype):
            return w_int.astype(dtype) * jnp.asarray(SCALE, dtype)
        wg = _dequant(w_gate, x.dtype)
        wu = _dequant(w_up, x.dtype)
        wd = _dequant(w_down, x.dtype)
        gate = jnp.einsum('bsd,hd->bsh', x, wg)
        up = jnp.einsum('bsd,hd->bsh', x, wu)
        h = jax.nn.silu(gate) * up
        return jnp.einsum('bsh,dh->bsd', h, wd)
    x = L0_attn_x
    x = _layernorm(x + _L0_attn_ref(x, L0_attn_w_qkv, L0_attn_w_swiglu, L0_attn_w_out), axis=-1)
    x = _layernorm(x + _L0_ffn_ref(x, L0_ffn_w_gate, L0_ffn_w_up, L0_ffn_w_down), axis=-1)
    return x

_drawn_inputs = setup_inputs


def setup_inputs(seed=0):
    import zlib

    import numpy as np

    out = dict(_drawn_inputs(seed))
    spreads = {}
    factors = {'L0_attn_w_qkv': 2.694}
    for name, (base, spread) in spreads.items():
        noise = np.random.default_rng([zlib.crc32(name.encode()), seed]).standard_normal(out[name].shape)
        drawn = base * np.exp(spread * noise) if base else spread * noise
        out[name] = jnp.asarray(drawn.astype(out[name].dtype))
    for name, factor in factors.items():
        out[name] = (out[name] * factor).astype(out[name].dtype)
    return out
```

```python
import concourse.bass as bass
from concourse import mybir
from contextlib import ExitStack

FP32 = mybir.dt.float32
FP16 = mybir.dt.float16
BF16 = mybir.dt.bfloat16
INT32 = mybir.dt.int32
ALU = mybir.AluOpType
ACT = mybir.ActivationFunctionType

P = 128
D = 256
KC = D // P
GT = 512
TT = GT // P
HID = 768
HC = HID // P
QKV = 3 * D
RMS_EPS = 1.1920929e-07
LN_EPS = 1e-5
CUM_EPS = 1e-6
WS = 256.0
DEQ = 1.0 / 127.0
CONSTS = 3
H_SLOTS = 3


def post_ln_layer_kernel(nc, x, w_qkv_t, w_swiglu_t, w_out_t, w_gate_t, w_up_t, w_down_t, out, seq_len):
    n_tokens = x.shape[0]
    NG = n_tokens // GT
    assert seq_len == 2 * GT and NG % 2 == 0 and NG >= 6

    x_g = x.rearrange("(g t p) d -> g p t d", t=TT, p=P)
    out_g = out.rearrange("(g t p) d -> g p t d", t=TT, p=P)

    ctx = ExitStack()
    with ctx:
        def sb(name, shape, dt=FP32):
            return ctx.enter_context(nc.sbuf_tensor(name, shape, dt))

        def sem(name):
            return ctx.enter_context(nc.semaphore(name))

        qkv_hi = sb("qkv_hi", [P, KC, QKV], FP16)
        qkv_lo = sb("qkv_lo", [P, KC, QKV], FP16)
        swi_hi = sb("swi_hi", [P, KC, 2 * D], FP16)
        swi_lo = sb("swi_lo", [P, KC, 2 * D], FP16)
        wo_hi = sb("wo_hi", [P, KC, D], FP16)
        wo_lo = sb("wo_lo", [P, KC, D], FP16)
        gate_w = sb("gate_w", [P, KC, HID], FP16)
        up_w = sb("up_w", [P, KC, HID], FP16)
        down_w = sb("down_w", [P, HC, D], FP16)
        ident = sb("ident", [P, P])
        ones = sb("ones", [P, GT])
        neg_half = sb("neg_half", [P, 8])
        eps_qk = sb("eps_qk", [P, 2])
        eps_x = sb("eps_x", [P, TT])
        x_in = sb("x_in", [P, 2, TT, D])
        xn = sb("xn", [P, 2, TT, D])
        xT_h = sb("xT_h", [P, KC, GT], FP16)
        xT_l = sb("xT_l", [P, KC, GT], FP16)
        ssx = sb("ssx", [P, 2, TT])
        argx = sb("argx", [P, TT])
        rx = sb("rx", [P, TT])
        junk_x = sb("junk_x", [P, TT, D], BF16)
        junk_qk = sb("junk_qk", [P, TT, 2, D], BF16)
        ssqk = sb("ssqk", [P, 2, TT, 2])
        argqk = sb("argqk", [P, TT, 2])
        rqk = sb("rqk", [P, TT, 2])
        tq = sb("tq", [P, TT, D])
        wk = sb("wk", [P, TT, D])
        kv = sb("kv", [P, TT, D])
        cum_w = sb("cum_w", [P, 2, KC, GT])
        cum_kv = sb("cum_kv", [P, 2, KC, GT])
        sig = sb("sig", [P, KC, GT])
        rec = sb("rec", [P, KC, GT])
        m_kv = sb("m_kv", [P, KC, GT])
        y = sb("y", [P, KC, GT])
        y_h = sb("y_h", [P, KC, GT], FP16)
        y_l = sb("y_l", [P, KC, GT], FP16)
        sil_g = sb("sil_g", [P, KC, GT])
        pr = sb("pr", [P, KC, GT])
        p_h = sb("p_h", [P, KC, GT], FP16)
        p_l = sb("p_l", [P, KC, GT], FP16)
        x_res = sb("x_res", [P, 2, TT, D])
        s1 = sb("s1", [P, TT, D])
        st1 = sb("st1", [P, TT, 6])
        mv1 = sb("mv1", [P, TT, 2])
        ve1 = sb("ve1", [P, TT])
        rstd1 = sb("rstd1", [P, TT])
        x1 = sb("x1", [P, 2, TT, D])
        x1T_h = sb("x1T_h", [P, KC, GT], FP16)
        x1T_l = sb("x1T_l", [P, KC, GT], FP16)
        sil_gate = sb("sil_gate", [P, H_SLOTS, GT])
        h = sb("h", [P, H_SLOTS, GT])
        h_h = sb("h_h", [P, HC, GT], FP16)
        h_l = sb("h_l", [P, HC, GT], FP16)
        s2 = sb("s2", [P, TT, D])
        st2 = sb("st2", [P, TT, 6])
        mv2 = sb("mv2", [P, TT, 2])
        ve2 = sb("ve2", [P, TT])
        rstd2 = sb("rstd2", [P, TT])
        nmr2 = sb("nmr2", [P, TT])
        o_sb = sb("o_sb", [P, 2, TT, D])
        qkv_st = cum_w[:, :, :, :].rearrange("p a b c -> p (a b c)")[:, 0:KC * QKV].rearrange(
            "p (c n) -> p c n", c=KC)
        swi_st = cum_kv[:, :, :, :].rearrange("p a b c -> p (a b c)")[:, 0:KC * 2 * D].rearrange(
            "p (c n) -> p c n", c=KC)
        wo_st = cum_kv[:, :, :, :].rearrange("p a b c -> p (a b c)")[:, KC * 2 * D:KC * 3 * D].rearrange(
            "p (c n) -> p c n", c=KC)
        gate_st = sb("gate_st", [P, KC, HID], INT32)
        up_st = sb("up_st", [P, KC, HID], INT32)
        down_st = sb("down_st", [P, HC, D], INT32)

        ps = ctx.enter_context(nc.psum_tensor("ps", [P, 8, GT], FP32))

        def bank(pair, half):
            return ps[:, 2 * pair + half, :]

        XT, WKV, TQ = 2, (3, 0), 1
        A_PAIR, D_PAIR, B_PAIR = (2, 3, 0, 1), (2, 3, 0, 3, 0, 1), (1, 2)
        C_PAIR, E_PAIR, X1T = 2, 0, 1

        w_in = {n: sem(f"{n}_loaded") for n in ("qkv", "swi", "wo", "gate", "up", "down")}
        x_loaded = [sem("x_loaded0"), sem("x_loaded1")]
        xres_loaded = [sem("xres_loaded0"), sem("xres_loaded1")]
        stored = [sem("stored0"), sem("stored1")]
        const_step = sem("const_step")
        qkv_split = sem("qkv_split")
        swi_hi_done = sem("swi_hi_done")
        swi_split = sem("swi_split")
        ffn_cast = sem("ffn_cast")
        ssx_ready = sem("ssx_ready")
        argx_ready = sem("argx_ready")
        rx_ready = sem("rx_ready")
        xn_ready = sem("xn_ready")
        xT_filled = sem("xT_filled")
        xT_hi = sem("xT_hi")
        xT_lo = sem("xT_lo")
        qkv_filled = sem("qkv_filled")
        ssqk_ready = sem("ssqk_ready")
        argqk_ready = sem("argqk_ready")
        rqk_ready = sem("rqk_ready")
        w_ready = sem("w_ready")
        kv_ready = sem("kv_ready")
        wkvT_filled = sem("wkvT_filled")
        tT_filled = sem("tT_filled")
        sig_ready = sem("sig_ready")
        scan_done = sem("scan_done")
        rec_ready = sem("rec_ready")
        m_ready = sem("m_ready")
        y_ready = sem("y_ready")
        y_hi = sem("y_hi")
        y_lo = sem("y_lo")
        ug_filled = sem("ug_filled")
        silg_ready = sem("silg_ready")
        p_ready = sem("p_ready")
        p_hi = sem("p_hi")
        p_lo = sem("p_lo")
        o_filled = sem("o_filled")
        s1_ready = sem("s1_ready")
        st1_ready = sem("st1_ready")
        mv1_ready = sem("mv1_ready")
        ve1_ready = sem("ve1_ready")
        rstd1_ready = sem("rstd1_ready")
        x1_ready = sem("x1_ready")
        x1T_filled = sem("x1T_filled")
        x1T_hi = sem("x1T_hi")
        x1T_lo = sem("x1T_lo")
        gu_filled = sem("gu_filled")
        silgate_ready = sem("silgate_ready")
        h_ready = sem("h_ready")
        h_hi = sem("h_hi")
        h_lo = sem("h_lo")
        f_filled = sem("f_filled")
        s2_ready = sem("s2_ready")
        st2_ready = sem("st2_ready")
        mv2_ready = sem("mv2_ready")
        ve2_ready = sem("ve2_ready")
        rstd2_ready = sem("rstd2_ready")
        nmr2_ready = sem("nmr2_ready")
        out_ready = sem("out_ready")

        def is_group(g):
            return not isinstance(g, int) or 0 <= g < NG

        def wait(eng, semaphore, value):
            if not isinstance(value, int) or value > 0:
                eng.wait_ge(semaphore, value)

        def run_steps(eng, step, first, ahead):
            pairs = (NG - ahead - 3) // 2
            for n in range(first, 3):
                step(n, n % 2)
            with eng.Fori(0, pairs) as i:
                step(2 * i + 3, 1)
                step(2 * i + 4, 0)
            for n in range(2 * pairs + 3, NG + 1):
                step(n, n % 2)

        block = ctx.enter_context(nc.Block())

        @block.sync
        def _(sp):
            def load_x_in(g, s):
                wait(sp, xn_ready, g - 1)
                sp.dma_start(x_in[:, s, :, :], x_g[g]).then_inc(x_loaded[s], 16)

            def load_x_res(g, s):
                wait(sp, s1_ready, 2 * (g - 1))
                sp.dma_start(x_res[:, s, :, :], x_g[g]).then_inc(xres_loaded[s], 16)

            def load_w(name, dst, src, chunks):
                sp.dma_start(dst, src.rearrange("(c p) n -> p c n", c=chunks)).then_inc(w_in[name], 16)

            load_x_in(0, 0)
            load_w("qkv", qkv_st, w_qkv_t, KC)
            load_x_in(1, 1)
            load_w("swi", swi_st, w_swiglu_t, KC)
            load_w("wo", wo_st, w_out_t, KC)
            load_w("gate", gate_st[:, :, :], w_gate_t, KC)
            load_w("up", up_st[:, :, :], w_up_t, KC)
            load_w("down", down_st[:, :, :], w_down_t, HC)

            def step(n, par):
                odd = 1 - par
                if is_group(n + 3):
                    load_x_in(n + 3, odd)
                if is_group(n + 1):
                    load_x_res(n + 1, odd)
                if is_group(n - 1):
                    wait(sp, out_ready, n)
                    sp.dma_start(out_g[n - 1], o_sb[:, odd, :, :]).then_inc(stored[odd], 16)

            run_steps(sp, step, -1, 3)
            for s in range(2):
                sp.wait_ge(stored[s], 16 * (NG // 2))

        @block.tensor
        def _(pe):
            mm = nc.tensor.matmul

            def x_transposed(g, par):
                wait(pe, xn_ready, g + 1)
                for c in range(KC):
                    if c == 0:
                        wait(pe, s1_ready, 2 * (g - 1))
                        if isinstance(g, int) and g == 1:
                            pe.wait_ge(kv_ready, 1)
                    for t in range(TT):
                        last = nc.tensor.transpose(bank(XT, c)[:, t * P:(t + 1) * P],
                                                   xn[:, par, t, c * P:(c + 1) * P], ident[:, :])
                    last.then_inc(xT_filled, 1)

            def wkv_transposed(g):
                wait(pe, kv_ready, 4 * g + 4)
                for c in range(KC):
                    if c == 0:
                        wait(pe, h_ready, 6 * (g - 2) + 4)
                    else:
                        wait(pe, s2_ready, 2 * (g - 1))
                    for half, src in enumerate((wk, kv)):
                        for t in range(TT):
                            last = nc.tensor.transpose(bank(WKV[c], half)[:, t * P:(t + 1) * P],
                                                       src[:, t, c * P:(c + 1) * P], ident[:, :])
                        last.then_inc(wkvT_filled, 1)
                wait(pe, x1T_lo, 2 * g)
                for c in range(KC):
                    for t in range(TT):
                        last = nc.tensor.transpose(bank(TQ, c)[:, t * P:(t + 1) * P],
                                                   tq[:, t, c * P:(c + 1) * P], ident[:, :])
                    last.then_inc(tT_filled, 1)

            def stage_a(g):
                wait(pe, xT_lo, 2 * g + 2)
                if isinstance(g, int) and g == 0:
                    pe.wait_ge(qkv_split, 4)
                for t in range(TT):
                    if t == 1:
                        wait(pe, scan_done, 4 * g - 2)
                    if t == 2:
                        wait(pe, scan_done, 4 * g)
                    if t == 3:
                        wait(pe, sig_ready, 2 * g)
                    qk, v = bank(A_PAIR[t], 0), bank(A_PAIR[t], 1)[:, 0:D]
                    cols = slice(t * P, (t + 1) * P)
                    for c in range(KC):
                        for part, w, first, final in ((xT_h, qkv_hi, c == 0, False), (xT_h, qkv_lo, False, False),
                                                      (xT_l, qkv_hi, False, c == KC - 1)):
                            mm(qk, part[:, c, cols], w[:, c, 0:2 * D], start=first, stop=final)
                            last = mm(v, part[:, c, cols], w[:, c, 2 * D:QKV], start=first, stop=final)
                    last.then_inc(qkv_filled, 1)

            def stage_b(g):
                if isinstance(g, int) and g == 0:
                    pe.wait_ge(swi_split, 2)
                for j in range(KC):
                    if j == 0 and is_group(g + 1):
                        wait(pe, kv_ready, 4 * g + 8)
                    if j == 0 and not is_group(g + 1):
                        wait(pe, sig_ready, 2 * g + 2)
                    if j == 1:
                        wait(pe, h_ready, 6 * g - 5)
                    for c in range(KC):
                        if j == 0:
                            wait(pe, y_lo, 2 * g + c + 1)
                        for half in range(2):
                            col = half * D + j * P
                            dst = bank(B_PAIR[j], half)
                            mm(dst, swi_hi[:, c, col:col + P], y_h[:, c, :], start=(c == 0), stop=False)
                            mm(dst, swi_hi[:, c, col:col + P], y_l[:, c, :], start=False, stop=False)
                            last = mm(dst, swi_lo[:, c, col:col + P], y_h[:, c, :], start=False, stop=(c == KC - 1))
                    last.then_inc(ug_filled, 1)

            def stage_c(g):
                wait(pe, p_lo, 2 * g + 2)
                for t in range(TT):
                    dst = bank(C_PAIR, t // 2)[:, (t % 2) * D:(t % 2 + 1) * D]
                    cols = slice(t * P, (t + 1) * P)
                    for c in range(KC):
                        mm(dst, p_h[:, c, cols], wo_hi[:, c, :], start=(c == 0), stop=False)
                        mm(dst, p_h[:, c, cols], wo_lo[:, c, :], start=False, stop=False)
                        last = mm(dst, p_l[:, c, cols], wo_hi[:, c, :], start=False, stop=(c == KC - 1))
                    if t % 2:
                        last.then_inc(o_filled, 1)

            def x1_transposed(g, par):
                wait(pe, x1_ready, g + 1)
                wait(pe, h_ready, 6 * g)
                for c in range(KC):
                    for t in range(TT):
                        last = nc.tensor.transpose(bank(X1T, c)[:, t * P:(t + 1) * P],
                                                   x1[:, par, t, c * P:(c + 1) * P], ident[:, :])
                    last.then_inc(x1T_filled, 1)

            def stage_d(g, chunks):
                for j in chunks:
                    if j == 0:
                        wait(pe, x1T_lo, 2 * g + 2)
                        if isinstance(g, int) and g == 0:
                            pe.wait_ge(ffn_cast, 3)
                    if j < 3 and is_group(g + 2):
                        wait(pe, kv_ready, 4 * (g + 2) + j + 1)
                    elif j == 0:
                        wait(pe, s1_ready, 2 * (g + 1))
                    elif j < 3 and is_group(g + 1):
                        wait(pe, scan_done, 4 * (g + 1) + 2 * j)
                    elif j == 1:
                        wait(pe, h_ready, 6 * (g - 1) + 4)
                    elif j == 2:
                        wait(pe, s2_ready, 2 * g)
                    elif j in (3, 4):
                        wait(pe, h_ready, 6 * g + j - 1)
                    elif is_group(g + 1):
                        wait(pe, p_ready, 2 * (g + 1) + 1)
                    for half, w in enumerate((gate_w, up_w)):
                        dst = bank(D_PAIR[j], half)
                        for c in range(KC):
                            mm(dst, w[:, c, j * P:(j + 1) * P], x1T_h[:, c, :], start=(c == 0), stop=False)
                            last = mm(dst, w[:, c, j * P:(j + 1) * P], x1T_l[:, c, :], start=False,
                                      stop=(c == KC - 1))
                    last.then_inc(gu_filled, 1)

            def stage_e(g):
                wait(pe, h_lo, 6 * g + 6)
                for t in range(TT):
                    dst = bank(E_PAIR, t // 2)[:, (t % 2) * D:(t % 2 + 1) * D]
                    cols = slice(t * P, (t + 1) * P)
                    for j in range(HC):
                        mm(dst, h_h[:, j, cols], down_w[:, j, :], start=(j == 0), stop=False)
                        last = mm(dst, h_l[:, j, cols], down_w[:, j, :], start=False, stop=(j == HC - 1))
                    if t % 2:
                        last.then_inc(f_filled, 1)

            def step(n, par):
                if is_group(n + 1):
                    x_transposed(n + 1, 1 - par)
                if is_group(n):
                    wkv_transposed(n)
                if is_group(n + 1):
                    stage_a(n + 1)
                if is_group(n - 1):
                    stage_d(n - 1, range(0, 3))
                if is_group(n):
                    stage_b(n)
                if is_group(n - 1):
                    stage_d(n - 1, range(3, 6))
                if is_group(n):
                    stage_c(n)
                if is_group(n - 1):
                    stage_e(n - 1)
                if is_group(n):
                    x1_transposed(n, par)

            pe.wait_ge(const_step, 2)
            run_steps(pe, step, -1, 1)

        @block.scalar
        def _(act):
            def x_squares(g, par):
                act.wait_ge(x_loaded[par], x_load_count(g, par))
                wait(act, ssx_ready, g)
                for t in range(TT):
                    last = nc.scalar.activation(junk_x[:, t, :], x_in[:, par, t, :], ACT.Square, scale=D ** -0.5,
                                                accum_out=ssx[:, par, t:t + 1])
                last.then_inc(ssx_ready, 1)

            def x_normed(g, par):
                wait(act, xT_filled, 2 * (g - 1))
                wait(act, rx_ready, g + 1)
                for t in range(TT):
                    last = nc.scalar.activation(xn[:, par, t, :], x_in[:, par, t, :], ACT.Copy, scale=rx[:, t:t + 1])
                last.then_inc(xn_ready, 1)

            def xT_hi_parts(g):
                wait(act, qkv_filled, 4 * g)
                for c in range(KC):
                    wait(act, xT_filled, 2 * g + c + 1)
                    nc.scalar.copy(xT_h[:, c, :], bank(XT, c)).then_inc(xT_hi, 1)

            def sigmoid_q(g):
                wait(act, m_ready, 2 * g)
                for c in range(KC):
                    wait(act, tT_filled, 2 * g + c + 1)
                    nc.scalar.activation(sig[:, c, :], bank(TQ, c), ACT.Copy, scale=0.5 / WS,
                                         bias=0.5 / WS).then_inc(sig_ready, 1)

            def qk_squares(g, t, par):
                wait(act, qkv_filled, 4 * g + t + 1)
                if t == 0:
                    wait(act, ssqk_ready, 4 * g)
                qk = bank(A_PAIR[t], 0)
                nc.scalar.activation(junk_qk[:, t, 0, :], qk[:, 0:D], ACT.Square, scale=2 * D ** -0.5,
                                     accum_out=ssqk[:, par, t, 0:1])
                nc.scalar.activation(junk_qk[:, t, 1, :], qk[:, D:2 * D], ACT.Square, scale=D ** -0.5,
                                     accum_out=ssqk[:, par, t, 1:2]).then_inc(ssqk_ready, 1)

            def tanh_exp(g, t):
                if t == 0:
                    wait(act, tT_filled, 2 * g)
                wait(act, rqk_ready, 4 * g + t + 1)
                qk = bank(A_PAIR[t], 0)
                nc.scalar.activation(tq[:, t, :], qk[:, 0:D], ACT.Tanh, scale=rqk[:, t, 0:1])
                nc.scalar.activation(wk[:, t, :], qk[:, D:2 * D], ACT.Exp, scale=rqk[:, t, 1:2]).then_inc(w_ready, 1)

            def y_hi_parts(g):
                wait(act, ug_filled, 2 * g)
                for c in range(KC):
                    wait(act, y_ready, 2 * g + c + 1)
                    nc.scalar.copy(y_h[:, c, :], y[:, c, :]).then_inc(y_hi, 1)

            def silu_gate(g, j):
                wait(act, gu_filled, 6 * g + j + 1)
                wait(act, h_ready, 6 * g + j + 1 - H_SLOTS)
                nc.scalar.activation(sil_gate[:, j % H_SLOTS, :], bank(D_PAIR[j], 0), ACT.Silu,
                                     scale=DEQ).then_inc(silgate_ready, 1)

            def h_hi_part(g, j):
                if j == 0:
                    wait(act, f_filled, 2 * g)
                wait(act, h_ready, 6 * g + j + 1)
                nc.scalar.copy(h_h[:, j, :], h[:, j % H_SLOTS, :]).then_inc(h_hi, 1)

            def silu_g(g, j):
                wait(act, ug_filled, 2 * g + j + 1)
                wait(act, p_ready, 2 * g)
                nc.scalar.activation(sil_g[:, j, :], bank(B_PAIR[j], 1), ACT.Silu, scale=1 / WS).then_inc(silg_ready, 1)

            def p_hi_part(g, j):
                if j == 0:
                    wait(act, o_filled, 2 * g)
                wait(act, p_ready, 2 * g + j + 1)
                nc.scalar.copy(p_h[:, j, :], pr[:, j, :]).then_inc(p_hi, 1)

            def x1T_hi_parts(g):
                wait(act, gu_filled, 6 * g)
                for c in range(KC):
                    wait(act, x1T_filled, 2 * g + c + 1)
                    nc.scalar.copy(x1T_h[:, c, :], bank(X1T, c)).then_inc(x1T_hi, 1)

            def out_norm(g, par):
                wait(act, nmr2_ready, g + 1)
                wait(act, stored[par], x_load_count(g, par) - 16)
                for t in range(TT):
                    last = nc.scalar.activation(o_sb[:, par, t, :], s2[:, t, :], ACT.Identity,
                                                bias=nmr2[:, t:t + 1], scale=rstd2[:, t:t + 1])
                last.then_inc(out_ready, 1)

            def step(n, par):
                odd = 1 - par
                if is_group(n + 1):
                    xT_hi_parts(n + 1)
                if is_group(n):
                    sigmoid_q(n)
                if is_group(n + 1):
                    qk_squares(n + 1, 0, odd)
                    qk_squares(n + 1, 1, odd)
                    tanh_exp(n + 1, 0)
                    qk_squares(n + 1, 2, odd)
                    tanh_exp(n + 1, 1)
                    qk_squares(n + 1, 3, odd)
                    tanh_exp(n + 1, 2)
                    tanh_exp(n + 1, 3)
                if is_group(n + 2):
                    x_squares(n + 2, par)
                if is_group(n):
                    y_hi_parts(n)
                if is_group(n - 1):
                    silu_gate(n - 1, 0)
                    silu_gate(n - 1, 1)
                    h_hi_part(n - 1, 0)
                    silu_gate(n - 1, 2)
                    h_hi_part(n - 1, 1)
                if is_group(n):
                    silu_g(n, 0)
                    silu_g(n, 1)
                    p_hi_part(n, 0)
                    p_hi_part(n, 1)
                if is_group(n - 1):
                    h_hi_part(n - 1, 2)
                    silu_gate(n - 1, 3)
                    silu_gate(n - 1, 4)
                    h_hi_part(n - 1, 3)
                    silu_gate(n - 1, 5)
                    h_hi_part(n - 1, 4)
                    h_hi_part(n - 1, 5)
                if is_group(n):
                    x1T_hi_parts(n)
                if is_group(n + 2):
                    x_normed(n + 2, par)
                if is_group(n - 1):
                    out_norm(n - 1, odd)

            step(-2, 0)
            step(-1, 1)
            act.wait_ge(w_in["swi"], 16)
            nc.scalar.mul(swi_hi[:, :, :], swi_st, WS)
            act.wait_ge(w_in["wo"], 16)
            nc.scalar.mul(wo_hi[:, :, :], wo_st, WS).then_inc(swi_hi_done, 1)
            for name, dst, src in (("gate", gate_w, gate_st), ("up", up_w, up_st), ("down", down_w, down_st)):
                act.wait_ge(w_in[name], 16)
                nc.scalar.copy(dst[:, :, :], src[:, :, :]).then_inc(ffn_cast, 1)
            run_steps(act, step, 0, 2)

        @block.vector
        def _(dve):
            def xT_lo_parts(g):
                wait(dve, qkv_filled, 4 * g)
                for c in range(KC):
                    wait(dve, xT_hi, 2 * g + c + 1)
                    nc.vector.tensor_sub(xT_l[:, c, :], bank(XT, c), xT_h[:, c, :]).then_inc(xT_lo, 1)

            def scans(g, par):
                wait(dve, m_ready, 2 * (g - 1))
                wait(dve, scan_done, 4 * g)
                for c in range(KC):
                    for half, cum in enumerate((cum_w, cum_kv)):
                        wait(dve, wkvT_filled, 4 * g + 2 * c + half + 1)
                        start = (CUM_EPS, 0.0)[half] if par == 0 else cum[:, 0, c, GT - 1:GT]
                        nc.vector.tensor_tensor_scan(cum[:, par, c, :], ones[:, :], bank(WKV[c], half), start,
                                                     ALU.mult, ALU.add).then_inc(scan_done, 1)

            def reciprocal_w(g, c, par):
                wait(dve, scan_done, 4 * g + 2 * c + 1)
                wait(dve, y_ready, 2 * (g - 1) + c + 1)
                nc.vector.reciprocal(rec[:, c, :], cum_w[:, par, c, :]).then_inc(rec_ready, 1)

            def y_chunk(g, c):
                wait(dve, m_ready, 2 * g + c + 1)
                wait(dve, rec_ready, 2 * g + c + 1)
                wait(dve, y_lo, 2 * (g - 1) + c + 1)
                nc.vector.tensor_mul(y[:, c, :], m_kv[:, c, :], rec[:, c, :]).then_inc(y_ready, 1)

            def kv_tile(g, t):
                if t == 0:
                    wait(dve, wkvT_filled, 4 * g)
                wait(dve, w_ready, 4 * g + t + 1)
                nc.vector.tensor_mul(kv[:, t, :], bank(A_PAIR[t], 1)[:, 0:D], wk[:, t, :]).then_inc(kv_ready, 1)

            def h_chunk(g, j):
                wait(dve, silgate_ready, 6 * g + j + 1)
                wait(dve, h_lo, 6 * g + j + 1 - H_SLOTS)
                nc.vector.scalar_tensor_tensor(h[:, j % H_SLOTS, :], bank(D_PAIR[j], 1), DEQ,
                                               sil_gate[:, j % H_SLOTS, :], ALU.mult, ALU.mult).then_inc(h_ready, 1)

            def h_lo_part(g, j):
                if j == 0:
                    wait(dve, f_filled, 2 * g)
                wait(dve, h_hi, 6 * g + j + 1)
                nc.vector.tensor_sub(h_l[:, j, :], h[:, j % H_SLOTS, :], h_h[:, j, :]).then_inc(h_lo, 1)

            def p_chunk(g, j):
                wait(dve, silg_ready, 2 * g + j + 1)
                wait(dve, p_lo, 2 * g)
                nc.vector.scalar_tensor_tensor(pr[:, j, :], bank(B_PAIR[j], 0), 1 / WS, sil_g[:, j, :],
                                               ALU.mult, ALU.mult).then_inc(p_ready, 1)

            def residual1(g, par):
                dve.wait_ge(xres_loaded[par], x_load_count(g, par))
                wait(dve, x1_ready, g)
                for q in range(2):
                    wait(dve, o_filled, 2 * g + q + 1)
                    nc.vector.scalar_tensor_tensor(
                        s1[:, 2 * q:2 * q + 2, :], bank(C_PAIR, q).rearrange("p (t d) -> p t d", t=2), 0.5 / WS,
                        x_res[:, par, 2 * q:2 * q + 2, :], ALU.mult, ALU.add).then_inc(s1_ready, 1)
                for t in range(TT):
                    wait(dve, s1_ready, 2 * g + t // 2 + 1)
                    last = nc.vector.bn_stats(st1[:, t, :], s1[:, t, :])
                last.then_inc(st1_ready, 1)
                dve.wait_ge(const_step, CONSTS)
                wait(dve, st1_ready, g + 1)
                for t in range(TT):
                    last = nc.vector.bn_aggr(mv1[:, t, :], st1[:, t, :])
                last.then_inc(mv1_ready, 1)
                wait(dve, mv1_ready, g + 1)
                wait(dve, rstd1_ready, g)
                nc.vector.tensor_scalar_add(ve1[:, :], mv1[:, :, 1], LN_EPS / 4).then_inc(ve1_ready, 1)

            def layernorm1(g, par):
                wait(dve, rstd1_ready, g + 1)
                wait(dve, x1T_filled, 2 * (g - 1))
                for t in range(TT):
                    last = nc.vector.tensor_scalar(x1[:, par, t, :], s1[:, t, :], mv1[:, t, 0:1], rstd1[:, t:t + 1],
                                                   ALU.subtract, ALU.mult)
                last.then_inc(x1_ready, 1)

            def residual2(g, par):
                wait(dve, out_ready, g)
                for q in range(2):
                    wait(dve, f_filled, 2 * g + q + 1)
                    nc.vector.scalar_tensor_tensor(
                        s2[:, 2 * q:2 * q + 2, :], bank(E_PAIR, q).rearrange("p (t d) -> p t d", t=2), DEQ,
                        x1[:, par, 2 * q:2 * q + 2, :], ALU.mult, ALU.add).then_inc(s2_ready, 1)
                for t in range(TT):
                    wait(dve, s2_ready, 2 * g + t // 2 + 1)
                    last = nc.vector.bn_stats(st2[:, t, :], s2[:, t, :])
                last.then_inc(st2_ready, 1)
                dve.wait_ge(const_step, CONSTS)
                wait(dve, st2_ready, g + 1)
                for t in range(TT):
                    last = nc.vector.bn_aggr(mv2[:, t, :], st2[:, t, :])
                last.then_inc(mv2_ready, 1)
                wait(dve, mv2_ready, g + 1)
                nc.vector.tensor_scalar_add(ve2[:, :], mv2[:, :, 1], LN_EPS).then_inc(ve2_ready, 1)

            def minus_mean_rstd(g):
                wait(dve, rstd2_ready, g + 1)
                nc.vector.scalar_tensor_tensor(nmr2[:, :], mv2[:, :, 0], -1.0, rstd2[:, :], ALU.mult,
                                               ALU.mult).then_inc(nmr2_ready, 1)

            def x1T_lo_parts(g):
                wait(dve, gu_filled, 6 * g)
                for c in range(KC):
                    wait(dve, x1T_hi, 2 * g + c + 1)
                    nc.vector.tensor_sub(x1T_l[:, c, :], bank(X1T, c), x1T_h[:, c, :]).then_inc(x1T_lo, 1)

            def step(n, par):
                odd = 1 - par
                before, now, after = is_group(n - 1), is_group(n), is_group(n + 1)
                if after:
                    xT_lo_parts(n + 1)
                if now:
                    scans(n, par)
                    reciprocal_w(n, 0, par)
                if after:
                    kv_tile(n + 1, 0)
                if now:
                    y_chunk(n, 0)
                if after:
                    kv_tile(n + 1, 1)
                if now:
                    reciprocal_w(n, 1, par)
                if after:
                    kv_tile(n + 1, 2)
                if now:
                    y_chunk(n, 1)
                if after:
                    kv_tile(n + 1, 3)
                if before:
                    h_chunk(n - 1, 0)
                    h_chunk(n - 1, 1)
                    h_lo_part(n - 1, 0)
                    h_chunk(n - 1, 2)
                    h_lo_part(n - 1, 1)
                if now:
                    p_chunk(n, 0)
                    p_chunk(n, 1)
                if before:
                    h_lo_part(n - 1, 2)
                    h_chunk(n - 1, 3)
                    h_chunk(n - 1, 4)
                    h_lo_part(n - 1, 3)
                    h_chunk(n - 1, 5)
                    h_lo_part(n - 1, 4)
                    h_lo_part(n - 1, 5)
                if now:
                    residual1(n, par)
                    layernorm1(n, par)
                if before:
                    residual2(n - 1, odd)
                if now:
                    x1T_lo_parts(n)
                if before:
                    minus_mean_rstd(n - 1)

            dve.wait_ge(w_in["qkv"], 16)
            for k, cols in enumerate((slice(0, 2 * D), slice(2 * D, QKV))):
                nc.vector.tensor_scalar_mul(qkv_hi[:, :, cols], qkv_st[:, :, cols], WS).then_inc(qkv_split, 1)
                dve.wait_ge(qkv_split, 2 * k + 1)
                nc.vector.scalar_tensor_tensor(qkv_lo[:, :, cols], qkv_st[:, :, cols], WS, qkv_hi[:, :, cols],
                                               ALU.mult, ALU.subtract).then_inc(qkv_split, 1)
            step(-1, 1)
            dve.wait_ge(swi_hi_done, 1)
            nc.vector.scalar_tensor_tensor(swi_lo[:, :, :], swi_st, WS, swi_hi[:, :, :], ALU.mult,
                                           ALU.subtract).then_inc(swi_split, 1)
            nc.vector.scalar_tensor_tensor(wo_lo[:, :, :], wo_st, WS, wo_hi[:, :, :], ALU.mult,
                                           ALU.subtract).then_inc(swi_split, 1)
            dve.wait_ge(swi_split, 2)
            dve.wait_ge(const_step, CONSTS)
            run_steps(dve, step, 0, 1)

        @block.gpsimd
        def _(pool):
            def rx_rows(g, par):
                wait(pool, ssx_ready, g + 1)
                nc.gpsimd.tensor_tensor(argx[:, :], ssx[:, par, :], eps_x[:, :], ALU.add).then_inc(argx_ready, 1)
                wait(pool, argx_ready, g + 1)
                nc.gpsimd.tensor_tensor(rx[:, :], argx[:, :], neg_half[:, 0:TT], ALU.pow).then_inc(rx_ready, 1)

            def rqk_tile(g, t, par):
                wait(pool, ssqk_ready, 4 * g + t + 1)
                nc.gpsimd.tensor_tensor(argqk[:, t, :], ssqk[:, par, t, :], eps_qk[:, :], ALU.add).then_inc(
                    argqk_ready, 1)
                wait(pool, argqk_ready, 4 * g + t + 1)
                nc.gpsimd.tensor_tensor(rqk[:, t, :], argqk[:, t, :], neg_half[:, 0:2], ALU.pow).then_inc(
                    rqk_ready, 1)

            def m_chunk(g, c, par):
                wait(pool, scan_done, 4 * g + 2 * c + 2)
                wait(pool, sig_ready, 2 * g + c + 1)
                wait(pool, y_ready, 2 * (g - 1) + c + 1)
                nc.gpsimd.tensor_mul(m_kv[:, c, :], cum_kv[:, par, c, :], sig[:, c, :]).then_inc(m_ready, 1)

            def y_lo_part(g, c):
                wait(pool, ug_filled, 2 * g)
                wait(pool, y_hi, 2 * g + c + 1)
                nc.gpsimd.tensor_sub(y_l[:, c, :], y[:, c, :], y_h[:, c, :]).then_inc(y_lo, 1)

            def p_lo_part(g, j):
                wait(pool, o_filled, 2 * g)
                wait(pool, p_hi, 2 * g + j + 1)
                nc.gpsimd.tensor_sub(p_l[:, j, :], pr[:, j, :], p_h[:, j, :]).then_inc(p_lo, 1)

            def rstd(g, ready, ve, dst, done):
                wait(pool, ready, g + 1)
                nc.gpsimd.tensor_tensor(dst[:, :], ve[:, :], neg_half[:, 0:TT], ALU.pow).then_inc(done, 1)

            def step(n, par):
                odd = 1 - par
                before, now, after = is_group(n - 1), is_group(n), is_group(n + 1)
                if now:
                    m_chunk(n, 0, par)
                if after:
                    rqk_tile(n + 1, 0, odd)
                if now:
                    m_chunk(n, 1, par)
                if after:
                    for t in range(1, TT):
                        rqk_tile(n + 1, t, odd)
                if is_group(n + 2):
                    rx_rows(n + 2, par)
                if now:
                    y_lo_part(n, 0)
                    y_lo_part(n, 1)
                    p_lo_part(n, 0)
                    p_lo_part(n, 1)
                if now:
                    rstd(n, ve1_ready, ve1, rstd1, rstd1_ready)
                if before:
                    rstd(n - 1, ve2_ready, ve2, rstd2, rstd2_ready)

            nc.gpsimd.memset(ident[:, :], 0.0).then_inc(const_step, 1)
            pool.wait_ge(const_step, 1)
            nc.gpsimd.affine_select(out=ident[:, :], in_=ident[:, :], compare_op=ALU.not_equal, fill=1.0, base=0,
                                    pattern=[[-1, P]], channel_multiplier=1).then_inc(const_step, 1)
            nc.gpsimd.memset(eps_qk[:, 0:1], 4 * RMS_EPS * WS * WS)
            nc.gpsimd.memset(eps_qk[:, 1:2], RMS_EPS * WS * WS)
            nc.gpsimd.memset(eps_x[:, :], RMS_EPS)
            nc.gpsimd.memset(neg_half[:, :], -0.5)
            nc.gpsimd.memset(ones[:, :], 1.0).then_inc(const_step, 1)
            pool.wait_ge(const_step, CONSTS)
            step(-2, 0)
            run_steps(pool, step, -1, 2)


def x_load_count(g, par):
    if isinstance(g, int):
        return 16 * (g // 2 + 1)
    return 8 * (g - par) + 16


def kernel(L0_attn_x, L0_attn_w_qkv, L0_attn_w_swiglu, L0_attn_w_out, L0_ffn_w_gate, L0_ffn_w_up, L0_ffn_w_down):
    import numpy as np
    import concourse.bacc as bacc
    from concourse.bass_utils import run_bass_kernel_spmd

    batch, seq_len, width = L0_attn_x.shape
    arrays = {
        "x": np.ascontiguousarray(L0_attn_x).reshape(batch * seq_len, width),
        "w_qkv_t": np.ascontiguousarray(np.asarray(L0_attn_w_qkv).T),
        "w_swiglu_t": np.ascontiguousarray(np.asarray(L0_attn_w_swiglu).T),
        "w_out_t": np.ascontiguousarray(np.asarray(L0_attn_w_out).T),
        "w_gate_t": np.ascontiguousarray(np.asarray(L0_ffn_w_gate).T),
        "w_up_t": np.ascontiguousarray(np.asarray(L0_ffn_w_up).T),
        "w_down_t": np.ascontiguousarray(np.asarray(L0_ffn_w_down).T),
    }
    nc = bacc.Bacc("TRN2", target_bir_lowering=False, num_devices=1)
    args = [nc.dram_tensor(name, a.shape, mybir.dt.from_np(a.dtype), kind="ExternalInput").ap()
            for name, a in arrays.items()]
    out = nc.dram_tensor("out", (batch * seq_len, width), FP32, kind="ExternalOutput").ap()
    post_ln_layer_kernel(nc, *args, out, seq_len)
    got = run_bass_kernel_spmd(nc, [arrays], core_ids=[0])
    return got.results[0]["out"].reshape(batch, seq_len, width)
```
